# Optimizing a Trainium2 kernel written in Bass

```python
import numpy as np
import jax
import jax.numpy as jnp

def _softmax(x, axis=-1):
    return jax.nn.softmax(x, axis=axis)

def _gelu(x):
    return jax.nn.gelu(x, approximate=True)

def _silu(x):
    return jax.nn.silu(x)

def _sigmoid(x):
    return jax.nn.sigmoid(x)

def _layernorm(x, axis=-1, eps=1e-05):
    m = jnp.mean(x, axis=axis, keepdims=True)
    v = jnp.var(x, axis=axis, keepdims=True)
    return (x - m) / jnp.sqrt(v + eps)

def _scatter_add(tgt, idx, src, axis=0):
    return tgt.at[idx].add(src)

def _segment_sum(src, seg, n):
    return jax.ops.segment_sum(src, seg, n)
kernel_name = 'mk_dlrm_tower_d1_rec_r8_63b9ea'

def setup_inputs(seed: int=0):
    np.random.seed(seed)
    _w = jnp.asarray

    def _rec_inputs():
        import jax
        import jax.numpy as jnp
        _tk = jax.random.key(seed)
        ids = jnp.stack([jax.random.randint(jax.random.fold_in(_tk, 200 + f), (2048,), 0, v, jnp.int32) for f, v in enumerate([12500, 125000, 12500, 12500, 12500, 1000, 12500, 12500, 1250, 12500, 12500, 1250, 1000, 1000, 1250, 12500, 1000, 1000, 1000, 1250, 1000, 1000, 1000, 1000, 1000, 1000])], axis=1)
        tbl_0 = 0.05 * jax.random.normal(jax.random.fold_in(_tk, 500 + 0), (12500, 128), jnp.float32)
        tbl_1 = 0.05 * jax.random.normal(jax.random.fold_in(_tk, 500 + 1), (125000, 128), jnp.float32)
        tbl_2 = 0.05 * jax.random.normal(jax.random.fold_in(_tk, 500 + 2), (12500, 128), jnp.float32)
        tbl_3 = 0.05 * jax.random.normal(jax.random.fold_in(_tk, 500 + 3), (12500, 128), jnp.float32)
        tbl_4 = 0.05 * jax.random.normal(jax.random.fold_in(_tk, 500 + 4), (12500, 128), jnp.float32)
        tbl_5 = 0.05 * jax.random.normal(jax.random.fold_in(_tk, 500 + 5), (1000, 128), jnp.float32)
        tbl_6 = 0.05 * jax.random.normal(jax.random.fold_in(_tk, 500 + 6), (12500, 128), jnp.float32)
        tbl_7 = 0.05 * jax.random.normal(jax.random.fold_in(_tk, 500 + 7), (12500, 128), jnp.float32)
        tbl_8 = 0.05 * jax.random.normal(jax.random.fold_in(_tk, 500 + 8), (1250, 128), jnp.float32)
        tbl_9 = 0.05 * jax.random.normal(jax.random.fold_in(_tk, 500 + 9), (12500, 128), jnp.float32)
        tbl_10 = 0.05 * jax.random.normal(jax.random.fold_in(_tk, 500 + 10), (12500, 128), jnp.float32)
        tbl_11 = 0.05 * jax.random.normal(jax.random.fold_in(_tk, 500 + 11), (1250, 128), jnp.float32)
        tbl_12 = 0.05 * jax.random.normal(jax.random.fold_in(_tk, 500 + 12), (1000, 128), jnp.float32)
        tbl_13 = 0.05 * jax.random.normal(jax.random.fold_in(_tk, 500 + 13), (1000, 128), jnp.float32)
        tbl_14 = 0.05 * jax.random.normal(jax.random.fold_in(_tk, 500 + 14), (1250, 128), jnp.float32)
        tbl_15 = 0.05 * jax.random.normal(jax.random.fold_in(_tk, 500 + 15), (12500, 128), jnp.float32)
        tbl_16 = 0.05 * jax.random.normal(jax.random.fold_in(_tk, 500 + 16), (1000, 128), jnp.float32)
        tbl_17 = 0.05 * jax.random.normal(jax.random.fold_in(_tk, 500 + 17), (1000, 128), jnp.float32)
        tbl_18 = 0.05 * jax.random.normal(jax.random.fold_in(_tk, 500 + 18), (1000, 128), jnp.float32)
        tbl_19 = 0.05 * jax.random.normal(jax.random.fold_in(_tk, 500 + 19), (1250, 128), jnp.float32)
        tbl_20 = 0.05 * jax.random.normal(jax.random.fold_in(_tk, 500 + 20), (1000, 128), jnp.float32)
        tbl_21 = 0.05 * jax.random.normal(jax.random.fold_in(_tk, 500 + 21), (1000, 128), jnp.float32)
        tbl_22 = 0.05 * jax.random.normal(jax.random.fold_in(_tk, 500 + 22), (1000, 128), jnp.float32)
        tbl_23 = 0.05 * jax.random.normal(jax.random.fold_in(_tk, 500 + 23), (1000, 128), jnp.float32)
        tbl_24 = 0.05 * jax.random.normal(jax.random.fold_in(_tk, 500 + 24), (1000, 128), jnp.float32)
        tbl_25 = 0.05 * jax.random.normal(jax.random.fold_in(_tk, 500 + 25), (1000, 128), jnp.float32)
        _rk = jax.random.fold_in(_tk, 7)
        r_dense_features = -0.000520686 + 1.00062 * jax.random.normal(jax.random.fold_in(_rk, 101), (2048, 128), jnp.float32)
        W_top1 = 0.0405887 * jax.random.normal(jax.random.fold_in(_tk, 801), (607, 512), jnp.float32)
        W_top2 = 0.0441942 * jax.random.normal(jax.random.fold_in(_tk, 802), (512, 256), jnp.float32)
        W_top3 = 0.0625 * jax.random.normal(jax.random.fold_in(_tk, 803), (256, 1), jnp.float32)
        b_top1 = jnp.zeros((512,), jnp.float32)
        b_top2 = jnp.zeros((256,), jnp.float32)
        return (r_dense_features, ids, tbl_0, tbl_1, tbl_2, tbl_3, tbl_4, tbl_5, tbl_6, tbl_7, tbl_8, tbl_9, tbl_10, tbl_11, tbl_12, tbl_13, tbl_14, tbl_15, tbl_16, tbl_17, tbl_18, tbl_19, tbl_20, tbl_21, tbl_22, tbl_23, tbl_24, tbl_25, W_top1, b_top1, W_top2, b_top2, W_top3)
    r_dense_features, ids, tbl_0, tbl_1, tbl_2, tbl_3, tbl_4, tbl_5, tbl_6, tbl_7, tbl_8, tbl_9, tbl_10, tbl_11, tbl_12, tbl_13, tbl_14, tbl_15, tbl_16, tbl_17, tbl_18, tbl_19, tbl_20, tbl_21, tbl_22, tbl_23, tbl_24, tbl_25, W_top1, b_top1, W_top2, b_top2, W_top3 = _rec_inputs()

    def _L0_rec_setup():
        import jax, jax.numpy as jnp
        import numpy as np
        F = 26
        N = F + 1
        _TRIU_I, _TRIU_J = np.triu_indices(N, k=1)
        key = jax.random.key(seed)
        k1, k2 = jax.random.split(key)
        B, D = (2048, 128)
        dense_features = jax.random.normal(k1, (B, D), dtype=jnp.float32)
        sparse_features = jax.random.normal(k2, (B, F, D), dtype=jnp.float32)
        return {'dense_features': dense_features, 'sparse_features': sparse_features}
    _L0_rec_all = _L0_rec_setup()
    _L0_rec_in = {k: v for k, v in _L0_rec_all.items() if k in ()}
    del _L0_rec_all
    return {'r_dense_features': r_dense_features, 'ids': ids, 'tbl_0': tbl_0, 'tbl_1': tbl_1, 'tbl_2': tbl_2, 'tbl_3': tbl_3, 'tbl_4': tbl_4, 'tbl_5': tbl_5, 'tbl_6': tbl_6, 'tbl_7': tbl_7, 'tbl_8': tbl_8, 'tbl_9': tbl_9, 'tbl_10': tbl_10, 'tbl_11': tbl_11, 'tbl_12': tbl_12, 'tbl_13': tbl_13, 'tbl_14': tbl_14, 'tbl_15': tbl_15, 'tbl_16': tbl_16, 'tbl_17': tbl_17, 'tbl_18': tbl_18, 'tbl_19': tbl_19, 'tbl_20': tbl_20, 'tbl_21': tbl_21, 'tbl_22': tbl_22, 'tbl_23': tbl_23, 'tbl_24': tbl_24, 'tbl_25': tbl_25, 'W_top1': W_top1, 'b_top1': b_top1, 'W_top2': W_top2, 'b_top2': b_top2, 'W_top3': W_top3}

def reference(r_dense_features, ids, tbl_0, tbl_1, tbl_2, tbl_3, tbl_4, tbl_5, tbl_6, tbl_7, tbl_8, tbl_9, tbl_10, tbl_11, tbl_12, tbl_13, tbl_14, tbl_15, tbl_16, tbl_17, tbl_18, tbl_19, tbl_20, tbl_21, tbl_22, tbl_23, tbl_24, tbl_25, W_top1, b_top1, W_top2, b_top2, W_top3):
    import jax
    import jax.numpy as jnp

    def _L0_rec_ref(dense_features, sparse_features):
        import jax, jax.numpy as jnp
        import numpy as np
        F = 26
        N = F + 1
        _TRIU_I, _TRIU_J = np.triu_indices(N, k=1)
        combined = jnp.concatenate([dense_features[:, None, :], sparse_features], axis=1)
        interactions = jnp.einsum('bnd,bmd->bnm', combined, combined)
        interactions_flat = interactions[:, _TRIU_I, _TRIU_J]
        return jnp.concatenate([dense_features, interactions_flat], axis=1)
    e = jnp.stack([tbl_0[ids[:, 0]], tbl_1[ids[:, 1]], tbl_2[ids[:, 2]], tbl_3[ids[:, 3]], tbl_4[ids[:, 4]], tbl_5[ids[:, 5]], tbl_6[ids[:, 6]], tbl_7[ids[:, 7]], tbl_8[ids[:, 8]], tbl_9[ids[:, 9]], tbl_10[ids[:, 10]], tbl_11[ids[:, 11]], tbl_12[ids[:, 12]], tbl_13[ids[:, 13]], tbl_14[ids[:, 14]], tbl_15[ids[:, 15]], tbl_16[ids[:, 16]], tbl_17[ids[:, 17]], tbl_18[ids[:, 18]], tbl_19[ids[:, 19]], tbl_20[ids[:, 20]], tbl_21[ids[:, 21]], tbl_22[ids[:, 22]], tbl_23[ids[:, 23]], tbl_24[ids[:, 24]], tbl_25[ids[:, 25]]], axis=1)
    z = _L0_rec_ref(r_dense_features, e)
    z = z.reshape(z.shape[0], -1)
    h = jnp.concatenate([z, r_dense_features], axis=1)
    h = jnp.maximum(h @ W_top1 + b_top1, 0.0)
    h = jnp.maximum(h @ W_top2 + b_top2, 0.0)
    y = h @ W_top3
    return y

_drawn_inputs = setup_inputs


def setup_inputs(seed=0):
    import zlib

    import numpy as np

    out = dict(_drawn_inputs(seed))
    spreads = {'b_top1': (0.0, 0.1), 'b_top2': (0.0, 0.1)}
    factors = {}
    for name, (base, spread) in spreads.items():
        noise = np.random.default_rng([zlib.crc32(name.encode()), seed]).standard_normal(out[name].shape)
        drawn = base * np.exp(spread * noise) if base else spread * noise
        out[name] = jnp.asarray(drawn.astype(out[name].dtype))
    for name, factor in factors.items():
        out[name] = (out[name] * factor).astype(out[name].dtype)
    return out
```

```python
import concourse.bass as bass
from concourse import mybir
from contextlib import ExitStack

BATCH, DIM = 2048, 128
ROWS = [12500, 125000, 12500, 12500, 12500, 1000, 12500, 12500, 1250, 12500, 12500, 1250, 1000,
        1000, 1250, 12500, 1000, 1000, 1000, 1250, 1000, 1000, 1000, 1000, 1000, 1000]
TABLES = len(ROWS)
FEATURES = TABLES + 1
HIDDEN1, HIDDEN2 = 512, 256

P = 128
TILE = 128
SLOTS = 2
TURN = SLOTS * TILE
TURNS = BATCH // TURN
QUAD = 32
QUADS = P // QUAD
GROUP = 4
GROUPS = -(-FEATURES // GROUP)
PAIR_ROWS = FEATURES - 1
PAIR_COLS = FEATURES - 1
ZCHUNKS = -(-PAIR_COLS // QUADS)
LAST_QUADS = PAIR_COLS - QUADS * (ZCHUNKS - 1)
BANK = 512
STEPS = TILE // QUADS
BANK_STEPS = STEPS // 2


def chunks_of_quadrant(q):
    return ZCHUNKS if q < LAST_QUADS else ZCHUNKS - 1


def members(g):
    return range(GROUP * g, min(GROUP * (g + 1), FEATURES))


def dlrm_tower(nc, dense, ids, tables, w_dense, w_pairs, b1, w2, b2, w3, out):
    fp32, i32 = mybir.dt.float32, mybir.dt.int32
    ALU, ACT = mybir.AluOpType, mybir.ActivationFunctionType
    K2, K3 = HIDDEN1 // P, HIDDEN2 // P

    with ExitStack() as ctx:
        def sb(name, shape, dt=fp32):
            return ctx.enter_context(nc.sbuf_tensor(name, shape, dt))

        def pb(name, shape):
            return ctx.enter_context(nc.psum_tensor(name, shape, fp32))

        def sem(name):
            return ctx.enter_context(nc.semaphore(name))

        ids_sb = sb("ids_sb", [P, SLOTS, TABLES], i32)
        rows = sb("rows", [P, SLOTS, FEATURES, DIM])
        cols = sb("cols", [P, SLOTS, TILE, FEATURES])
        dense_t = sb("dense_t", [P, SLOTS, TILE])
        z = sb("z", [P, ZCHUNKS, TURN])
        h1 = sb("h1", [P, K2, TURN])
        h2 = sb("h2", [P, K3, TURN])
        y = sb("y", [1, BATCH])
        ident = sb("ident", [P, P])
        wd2 = sb("wd2", [P, 2, HIDDEN1])
        wd = sb("wd", [P, HIDDEN1])
        wz = sb("wz", [P, ZCHUNKS, HIDDEN1])
        w2_sb = sb("w2_sb", [P, K2, HIDDEN2])
        w3_sb = sb("w3_sb", [P, K3])
        b1_sb = sb("b1_sb", [P, K2])
        b2_sb = sb("b2_sb", [P, K3])

        turned = [pb(f"turned{k}", [P, GROUP, TILE]) for k in range(2)]
        gram = [pb(f"gram{s}", [P, 2, BANK]) for s in range(SLOTS)]
        mlp = [pb(f"mlp{k}", [P, BANK]) for k in range(2)]

        ident_zeroed, ident_ready = sem("ident_zeroed"), sem("ident_ready")
        z_zeroed = sem("z_zeroed")
        loaded_wd, loaded_wz, loaded_w2 = sem("loaded_wd"), sem("loaded_wz"), sem("loaded_w2")
        loaded_small = sem("loaded_small")
        wd_summed = sem("wd_summed")
        ids_loaded = [sem(f"ids_loaded{s}") for s in range(SLOTS)]
        dense_loaded = [sem(f"dense_loaded{s}") for s in range(SLOTS)]
        gathered = [[sem(f"gathered{s}_{g}") for g in range(GROUPS)] for s in range(SLOTS)]
        gathers_begun = sem("gathers_begun")
        rows_used = [sem(f"rows_used{s}") for s in range(SLOTS)]
        group_turned = [sem(f"group_turned{k}") for k in range(2)]
        group_kept = [sem(f"group_kept{k}") for k in range(2)]
        gram_done = [sem(f"gram_done{s}") for s in range(SLOTS)]
        dense_kept = sem("dense_kept")
        z_by_dve, z_by_act = sem("z_by_dve"), sem("z_by_act")
        h1_product, h2_product, y_product = sem("h1_product"), sem("h2_product"), sem("y_product")
        h1_by_dve, h1_by_act = sem("h1_by_dve"), sem("h1_by_act")
        h2_by_dve, h2_by_act = sem("h2_by_dve"), sem("h2_by_act")
        y_kept, stored = sem("y_kept"), sem("stored")

        block = ctx.enter_context(nc.Block())

        def bank_of(s, g):
            return (GROUPS * s + g) % 2

        def use_of(s, g):
            return (GROUPS * s + g) // 2

        BANK_USES = SLOTS * GROUPS // 2
        assert SLOTS * GROUPS % 2 == 0

        def uses_until(s, k):
            return sum(bank_of(a, g) == k for a in range(s + 1) for g in range(GROUPS))

        def copies_of(engine):
            return [(a, b) for a in range(QUADS) if a % 2 == engine for b in range(QUADS)]

        Z_COPIES = len(copies_of(0))

        @block.sync
        def _(sp):
            def load(i, s):
                at = bass.ds(i * TURN + s * TILE, TILE)
                sp.dma_start(ids_sb[:, s, :], ids[at, :]).then_inc(ids_loaded[s], 16)
                sp.dma_start(rows[:, s, 0, :], dense[at, :]).then_inc(dense_loaded[s], 16)

            for s in range(SLOTS):
                load(0, s)
            with sp.Fori(1, TURNS) as i:
                for s in range(SLOTS):
                    sp.wait_ge(rows_used[s], i)
                    load(i, s)
            sp.wait_ge(y_kept, TURNS)
            sp.dma_start(out, y[:, :]).then_inc(stored, 16)
            sp.wait_ge(stored, 16)

        @block.gpsimd
        def _(pool):
            pool.memset(ident[:, :], 0.0).then_inc(ident_zeroed, 1)
            pool.wait_ge(ident_zeroed, 1)
            pool.affine_select(out=ident[:, :], in_=ident[:, :], compare_op=ALU.not_equal, fill=1.0,
                               base=0, pattern=[[-1, P]], channel_multiplier=1).then_inc(ident_ready, 1)

            def gather(s):
                for g in range(GROUPS):
                    for n in members(g):
                        if n:
                            pool.indirect_dma_start(
                                out=rows[:, s, n, :], out_offset=None, in_=tables[n - 1],
                                in_offset=bass.IndirectOffsetOnAxis(ap=ids_sb[:, s, n - 1:n], axis=0),
                            ).then_inc(gathered[s][g], 16)

            for s in range(SLOTS):
                pool.wait_ge(ids_loaded[s], 16)
                gather(s)
            with pool.Fori(1, TURNS) as i:
                for s in range(SLOTS):
                    pool.wait_ge(rows_used[s], i)
                    pool.wait_ge(ids_loaded[s], i * 16 + 16)
                    pool.sem_inc(gathers_begun, 1)
                    gather(s)

        def keep_group(eng, copy, i, s, g):
            k, n = bank_of(s, g), members(g)
            eng.wait_ge(group_turned[k], i * BANK_USES + use_of(s, g) + 1)
            copy(cols[:, s, :, n[0]:n[-1] + 1].rearrange("p b n -> p n b"),
                 turned[k][:, 0:len(n), :]).then_inc(group_kept[k], 1)

        def keep_z(eng, copy, s, engine, done):
            for a, b in copies_of(engine):
                m = chunks_of_quadrant(b)
                src = gram[s][a * QUAD:a * QUAD + PAIR_ROWS, :, 0:BANK_STEPS * PAIR_COLS]
                src = src.rearrange("p h (t j) -> p h t j", j=PAIR_COLS)[:, :, :, b:b + QUADS * (m - 1) + 1:QUADS]
                at = s * TILE + a * STEPS
                dst = z[b * QUAD:b * QUAD + PAIR_ROWS, 0:m, at:at + STEPS]
                copy(dst.rearrange("p m (h t) -> p h t m", h=2), src).then_inc(done, 1)

        @block.vector
        def _(dve):
            dve.memset(z[:, :, :], 0.0).then_inc(z_zeroed, 1)
            dve.wait_ge(loaded_wd, 16)
            dve.tensor_tensor(wd[:, :], wd2[:, 0, :], wd2[:, 1, :], ALU.add).then_inc(wd_summed, 1)
            dve.wait_ge(loaded_small, 48)
            dve.wait_ge(z_zeroed, 1)

            def columns(i, s, first=False):
                if not first:
                    dve.wait_ge(gram_done[s], i)
                for g in range(GROUPS):
                    if bank_of(s, g) == 0:
                        keep_group(dve, dve.tensor_copy, i, s, g)

            def interactions(i, s):
                dve.wait_ge(gram_done[s], i + 1)
                dve.tensor_copy(dense_t[:, s, :], cols[:, s, :, 0]).then_inc(dense_kept, 1)
                keep_z(dve, dve.tensor_copy, s, 0, z_by_dve)

            def layer1(i):
                for c in range(1, K2, 2):
                    dve.wait_ge(h1_product, i * K2 + c + 1)
                    dve.tensor_scalar(h1[:, c, :], mlp[c % 2][:, c // 2 * TURN:c // 2 * TURN + TURN],
                                      b1_sb[:, c:c + 1], 0.0, ALU.add, ALU.max).then_inc(h1_by_dve, 1)

            def layer2(i):
                dve.wait_ge(h2_product, i * K3 + 2)
                dve.tensor_scalar(h2[:, 1, :], mlp[1][:, 0:TURN], b2_sb[:, 1:2], 0.0,
                                  ALU.add, ALU.max).then_inc(h2_by_dve, 1)

            def last(i):
                dve.wait_ge(y_product, i + 1)
                dve.tensor_copy(y[0:1, bass.ds(i * TURN, TURN)], mlp[0][0:1, TURN:2 * TURN]).then_inc(y_kept, 1)

            for s in range(SLOTS):
                columns(0, s, first=True)
                interactions(0, s)
            with dve.Fori(1, TURNS) as i:
                columns(i, 0)
                layer1(i - 1)
                interactions(i, 0)
                columns(i, 1)
                layer2(i - 1)
                interactions(i, 1)
                last(i - 1)
            layer1(TURNS - 1)
            layer2(TURNS - 1)
            last(TURNS - 1)

        @block.scalar
        def _(act):
            act.dma_start(b1_sb[:, :], b1).then_inc(loaded_small, 16)
            act.dma_start(b2_sb[:, :], b2).then_inc(loaded_small, 16)
            act.dma_start(w3_sb[:, :], w3).then_inc(loaded_small, 16)
            act.dma_start(wd2[:, :, :], w_dense).then_inc(loaded_wd, 16)
            act.dma_start(wz[:, :, :], w_pairs).then_inc(loaded_wz, 16)
            act.dma_start(w2_sb[:, :, :], w2).then_inc(loaded_w2, 16)
            act.wait_ge(loaded_small, 48)
            act.wait_ge(z_zeroed, 1)

            def copy(dst, src):
                return act.activation(dst, src, ACT.Copy)

            def columns(i, s, first=False):
                if not first:
                    act.wait_ge(gram_done[s], i)
                    act.wait_ge(dense_kept, (i - 1) * SLOTS + s + 1)
                for g in range(GROUPS):
                    if bank_of(s, g) == 1:
                        keep_group(act, copy, i, s, g)

            def interactions(i, s):
                act.wait_ge(gram_done[s], i + 1)
                keep_z(act, copy, s, 1, z_by_act)

            def layer1(i):
                for c in range(0, K2, 2):
                    act.wait_ge(h1_product, i * K2 + c + 1)
                    act.activation(h1[:, c, :], mlp[c % 2][:, c // 2 * TURN:c // 2 * TURN + TURN],
                                   ACT.Relu, bias=b1_sb[:, c:c + 1]).then_inc(h1_by_act, 1)

            def layer2(i):
                act.wait_ge(h2_product, i * K3 + 1)
                act.activation(h2[:, 0, :], mlp[0][:, 0:TURN], ACT.Relu,
                               bias=b2_sb[:, 0:1]).then_inc(h2_by_act, 1)

            for s in range(SLOTS):
                columns(0, s, first=True)
                interactions(0, s)
            with act.Fori(1, TURNS) as i:
                columns(i, 0)
                layer1(i - 1)
                interactions(i, 0)
                columns(i, 1)
                layer2(i - 1)
                interactions(i, 1)
            layer1(TURNS - 1)
            layer2(TURNS - 1)

        @block.tensor
        def _(pe):
            pe.wait_ge(ident_ready, 1)

            def turn_rows(i, s, first):
                for g in range(GROUPS):
                    k, n = bank_of(s, g), members(g)
                    if g == 0:
                        pe.wait_ge(dense_loaded[s], i * 16 + 16)
                    gathers = sum(f > 0 for f in n)
                    pe.wait_ge(gathered[s][g], i * (16 * gathers) + 16 * gathers)
                    if not first or use_of(s, g):
                        pe.wait_ge(group_kept[k], i * BANK_USES + use_of(s, g))
                    for f in n:
                        done = pe.transpose(turned[k][:, f - n[0], :], rows[:, s, f, :], ident[:, :])
                    done.then_inc(group_turned[k], 1)

            def gram_products(i, s, first):
                for k in range(2):
                    pe.wait_ge(group_kept[k], i * BANK_USES + uses_until(s, k))
                if not first:
                    pe.wait_ge(z_by_dve, (i - 1) * (SLOTS * Z_COPIES) + (s + 1) * Z_COPIES)
                    pe.wait_ge(z_by_act, (i - 1) * (SLOTS * Z_COPIES) + (s + 1) * Z_COPIES)
                for t in range(STEPS):
                    h, u = divmod(t, BANK_STEPS)
                    for a in range(QUADS):
                        of = cols[:, s, a * STEPS + t, :]
                        done = pe.matmul(gram[s][a * QUAD:a * QUAD + PAIR_ROWS, h, u * PAIR_COLS:(u + 1) * PAIR_COLS],
                                         of[:, 0:PAIR_ROWS], of[:, 1:FEATURES], start=True, stop=True)
                        if t == 0 and a == 0:
                            done.then_inc(rows_used[s], 1)
                done.then_inc(gram_done[s], 1)

            def layer1(i):
                pe.wait_ge(dense_kept, i * SLOTS + SLOTS)
                pe.wait_ge(z_by_dve, i * (SLOTS * Z_COPIES) + SLOTS * Z_COPIES)
                pe.wait_ge(z_by_act, i * (SLOTS * Z_COPIES) + SLOTS * Z_COPIES)
                for c in range(K2):
                    if c >= 2:
                        pe.wait_ge((h1_by_act, h1_by_dve)[c % 2], i * (K2 // 2) + c // 2)
                    to = mlp[c % 2][:, c // 2 * TURN:c // 2 * TURN + TURN]
                    n = slice(c * P, c * P + P)
                    pe.matmul(to, wd[:, n], dense_t[:, :, :].rearrange("p s b -> p (s b)"), start=True, stop=False)
                    for m in range(ZCHUNKS):
                        k = P if m < ZCHUNKS - 1 else LAST_QUADS * QUAD
                        done = pe.matmul(to, wz[0:k, m, n], z[0:k, m, :], start=False, stop=(m == ZCHUNKS - 1))
                    done.then_inc(h1_product, 1)

            def layer2(i):
                pe.wait_ge(h1_by_act, i * (K2 // 2) + K2 // 2)
                pe.wait_ge(h1_by_dve, i * (K2 // 2) + K2 // 2)
                for c in range(K3):
                    for m in range(K2):
                        done = pe.matmul(mlp[c][:, 0:TURN], w2_sb[:, m, c * P:c * P + P], h1[:, m, :],
                                         start=(m == 0), stop=(m == K2 - 1))
                    done.then_inc(h2_product, 1)

            def layer3(i):
                pe.wait_ge(h2_by_act, i + 1)
                pe.wait_ge(h2_by_dve, i + 1)
                for m in range(K3):
                    done = pe.matmul(mlp[0][0:1, TURN:2 * TURN], w3_sb[:, m:m + 1], h2[:, m, :],
                                     start=(m == 0), stop=(m == K3 - 1))
                done.then_inc(y_product, 1)

            for s in range(SLOTS):
                turn_rows(0, s, True)
                gram_products(0, s, True)
            pe.wait_ge(wd_summed, 1)
            pe.wait_ge(loaded_wz, 16)
            pe.wait_ge(loaded_w2, 16)
            pe.wait_ge(loaded_small, 48)
            with pe.Fori(1, TURNS) as i:
                turn_rows(i, 0, False)
                layer1(i - 1)
                gram_products(i, 0, False)
                turn_rows(i, 1, False)
                layer2(i - 1)
                gram_products(i, 1, False)
                layer3(i - 1)
                pe.wait_ge(y_kept, i)
            layer1(TURNS - 1)
            layer2(TURNS - 1)
            layer3(TURNS - 1)


def kernel(**inputs):
    import numpy as np
    import concourse.bacc as bacc
    from concourse.bass_utils import run_bass_kernel_spmd

    w_top1 = np.asarray(inputs["W_top1"])
    w_pairs = np.zeros((P, ZCHUNKS, HIDDEN1), w_top1.dtype)
    row = DIM
    for i in range(FEATURES):
        for j in range(i + 1, FEATURES):
            m, q = divmod(j - 1, QUADS)
            w_pairs[q * QUAD + i, m] = w_top1[row]
            row += 1
    arrays = {
        "dense": np.ascontiguousarray(inputs["r_dense_features"]),
        "ids": np.ascontiguousarray(inputs["ids"]),
        **{f"table{n}": np.ascontiguousarray(inputs[f"tbl_{n}"]) for n in range(TABLES)},
        "w_dense": np.ascontiguousarray(np.stack([w_top1[:DIM], w_top1[row:]], axis=1)),
        "w_pairs": w_pairs,
        "b1": np.ascontiguousarray(np.asarray(inputs["b_top1"]).reshape(-1, P).T),
        "w2": np.ascontiguousarray(np.asarray(inputs["W_top2"]).reshape(-1, P, HIDDEN2).transpose(1, 0, 2)),
        "b2": np.ascontiguousarray(np.asarray(inputs["b_top2"]).reshape(-1, P).T),
        "w3": np.ascontiguousarray(np.asarray(inputs["W_top3"]).reshape(-1, P).T),
    }
    nc = bacc.Bacc("TRN2", target_bir_lowering=False, num_devices=1)
    at = {name: nc.dram_tensor(name, a.shape, mybir.dt.from_np(a.dtype), kind="ExternalInput").ap()
          for name, a in arrays.items()}
    out = nc.dram_tensor("out", (1, BATCH), mybir.dt.float32, kind="ExternalOutput").ap()
    dlrm_tower(nc, at["dense"], at["ids"], [at[f"table{n}"] for n in range(TABLES)], at["w_dense"],
               at["w_pairs"], at["b1"], at["w2"], at["b2"], at["w3"], out)
    result = run_bass_kernel_spmd(nc, [arrays], core_ids=[0])
    return result.results[0]["out"].reshape(BATCH, 1)
```

```python
import concourse.bass as bass
from concourse import mybir
from contextlib import ExitStack

BATCH, DIM = 2048, 128
ROWS = [12500, 125000, 12500, 12500, 12500, 1000, 12500, 12500, 1250, 12500, 12500, 1250, 1000,
        1000, 1250, 12500, 1000, 1000, 1000, 1250, 1000, 1000, 1000, 1000, 1000, 1000]
TABLES = len(ROWS)
FEATURES = TABLES + 1
SMALL = 1000
PICKED = [n for n in range(TABLES) if ROWS[n] == SMALL][-6:]
GATHERED = [n for n in range(TABLES) if n not in PICKED]
ORDER = GATHERED + PICKED
HIDDEN1, HIDDEN2 = 512, 256

P = 128
TILE = 128
SLOTS = 2
TURN = SLOTS * TILE
TURNS = BATCH // TURN
QUAD = 32
QUADS = P // QUAD
GROUP = 4
ROW_FEATURES = 1 + len(GATHERED)
GROUPS = -(-ROW_FEATURES // GROUP)
PICKS = len(PICKED)
PICK_GROUP = 2
PICK_GROUPS = -(-PICKS // PICK_GROUP)
WHOLE = SMALL // P
REST = SMALL - WHOLE * P
PARTS = WHOLE + 1
RING = 3
PAIR_ROWS = FEATURES - 1
PAIR_COLS = FEATURES - 1
ZCHUNKS = -(-PAIR_COLS // QUADS)
LAST_QUADS = PAIR_COLS - QUADS * (ZCHUNKS - 1)
BANK = 512
STEPS = TILE // QUADS
BANK_STEPS = STEPS // 2


def chunks_of_quadrant(q):
    return ZCHUNKS if q < LAST_QUADS else ZCHUNKS - 1


def members(g):
    return range(GROUP * g, min(GROUP * (g + 1), ROW_FEATURES))


def picks(g):
    return range(PICK_GROUP * g, min(PICK_GROUP * (g + 1), PICKS))


def dlrm_tower(nc, dense, ids, picked_ids, tables, w_dense, w_pairs, b1, w2, b2, w3, out):
    fp32, fp32r, i32 = mybir.dt.float32, mybir.dt.float32r, mybir.dt.int32
    ALU, ACT = mybir.AluOpType, mybir.ActivationFunctionType
    K2, K3 = HIDDEN1 // P, HIDDEN2 // P

    with ExitStack() as ctx:
        def sb(name, shape, dt=fp32):
            return ctx.enter_context(nc.sbuf_tensor(name, shape, dt))

        def pb(name, shape):
            return ctx.enter_context(nc.psum_tensor(name, shape, fp32))

        def sem(name):
            return ctx.enter_context(nc.semaphore(name))

        ids_sb = sb("ids_sb", [P, SLOTS, len(GATHERED)], i32)
        rows = sb("rows", [P, SLOTS, ROW_FEATURES, DIM])
        raw = sb("raw", [P, 2, PARTS * DIM])
        table_hi = sb("table_hi", [P, PICKS, PARTS, DIM], fp32r)
        table_lo = sb("table_lo", [P, PICKS, PARTS, DIM], fp32r)
        row_int = sb("row_int", [P, PARTS], i32)
        row_number = sb("row_number", [P, PARTS])
        wanted = sb("wanted", [P, PICKS, TURN], i32)
        hot = sb("hot", [P, RING, PARTS, TURN], fp32r)
        cols = sb("cols", [P, SLOTS, TILE, FEATURES])
        dense_hi = sb("dense_hi", [P, SLOTS, TILE], fp32r)
        dense_lo = sb("dense_lo", [P, SLOTS, TILE], fp32r)
        z_raw = sb("z_raw", [P, ZCHUNKS, TILE])
        z_hi = sb("z_hi", [P, ZCHUNKS, TURN], fp32r)
        z_lo = sb("z_lo", [P, ZCHUNKS, TURN], fp32r)
        h1 = sb("h1", [P, K2, TURN])
        h2 = sb("h2", [P, K3, TURN])
        y = sb("y", [1, BATCH])
        ident = sb("ident", [P, P])
        wd_raw = sb("wd_raw", [P, HIDDEN1])
        wd_hi = sb("wd_hi", [P, HIDDEN1], fp32r)
        wd_lo = sb("wd_lo", [P, HIDDEN1], fp32r)
        wz_hi = sb("wz_hi", [P, ZCHUNKS, HIDDEN1], fp32r)
        wz_lo = sb("wz_lo", [P, ZCHUNKS, HIDDEN1], fp32r)
        w2_sb = sb("w2_sb", [P, K2, HIDDEN2])
        w3_sb = sb("w3_sb", [P, K3])
        b1_sb = sb("b1_sb", [P, K2])
        b2_sb = sb("b2_sb", [P, K3])

        turned = [pb(f"turned{k}", [P, GROUP, TILE]) for k in range(2)]
        gram = [pb(f"gram{s}", [P, 2, BANK]) for s in range(SLOTS)]
        mlp = [pb(f"mlp{k}", [P, BANK]) for k in range(2)]

        ident_zeroed, ident_ready = sem("ident_zeroed"), sem("ident_ready")
        rows_numbered, numbers_ready = sem("rows_numbered"), sem("numbers_ready")
        raw_loaded = [sem(f"raw_loaded{k}") for k in range(2)]
        raw_cleared = sem("raw_cleared")
        hi_ready, lo_ready = sem("hi_ready"), sem("lo_ready")
        wanted_loaded, hot_made, hot_used = sem("wanted_loaded"), sem("hot_made"), sem("hot_used")
        z_zeroed = sem("z_zeroed")
        loaded_w2 = sem("loaded_w2")
        loaded_small = sem("loaded_small")
        wd_summed = sem("wd_summed")
        ids_loaded = [sem(f"ids_loaded{s}") for s in range(SLOTS)]
        dense_loaded = [sem(f"dense_loaded{s}") for s in range(SLOTS)]
        gathered = [[sem(f"gathered{s}_{g}") for g in range(GROUPS)] for s in range(SLOTS)]
        gathers_begun = sem("gathers_begun")
        group_turned = [sem(f"group_turned{k}") for k in range(2)]
        group_kept = [sem(f"group_kept{k}") for k in range(2)]
        gram_done = [sem(f"gram_done{s}") for s in range(SLOTS)]
        dense_hi_kept, dense_kept = sem("dense_hi_kept"), sem("dense_kept")
        z_hi_kept, z_lo_kept = sem("z_hi_kept"), sem("z_lo_kept")
        z_by_dve, z_by_act = sem("z_by_dve"), sem("z_by_act")
        h1_product, h2_product, y_product = sem("h1_product"), sem("h2_product"), sem("y_product")
        h1_kept, h2_kept = sem("h1_kept"), sem("h2_kept")
        y_kept, stored = sem("y_kept"), sem("stored")

        block = ctx.enter_context(nc.Block())

        EARLY = PICK_GROUPS - 1
        assert PICKS <= PICK_GROUP * EARLY + RING

        USES = [("pick", g) for g in range(EARLY)] + [(0, g) for g in range(GROUPS)]
        USES += [("pick", g) for g in range(EARLY, PICK_GROUPS)] + [(1, g) for g in range(GROUPS)]
        BANK_USES = [len(USES[k::2]) for k in range(2)]

        def bank_of(s, g):
            return USES.index((s, g)) % 2

        def use_of(s, g):
            return USES.index((s, g)) // 2

        def uses_until(s, k):
            return len(USES[k:USES.index(("pick", PICK_GROUPS - 1) if s == 0 else (s, GROUPS - 1)) + 1:2])

        def turns_of_bank(s, g):
            k = bank_of(s, g)
            return sum(u[0] != "pick" for u in USES[k:USES.index((s, g)) + 1:2])

        BANK_TURNS = [sum(u[0] != "pick" for u in USES[k::2]) for k in range(2)]

        PIECES = ([("table", t) for t in range(PICKS)] + [("dense", 0)]
                  + [("pairs", m) for m in range(0, ZCHUNKS, 2)])
        loads = [32 if kind == "table" else 16 for kind, _ in PIECES]

        def loaded(n):
            return sum(loads[n % 2:n + 1:2])

        def of_raw(n):
            kind, at = PIECES[n]
            if kind == "table":
                return raw[:, n % 2, :].rearrange("p (c d) -> p c d", d=DIM), table_hi[:, at], table_lo[:, at]
            if kind == "dense":
                return wd_raw[:, :], wd_hi[:, :], wd_lo[:, :]
            m = min(2, ZCHUNKS - at)
            return (raw[:, n % 2, 0:m * HIDDEN1].rearrange("p (m n) -> p m n", m=m),
                    wz_hi[:, at:at + m, :], wz_lo[:, at:at + m, :])

        def wait_rows_turned(eng, i, s):
            eng.wait_ge(group_turned[bank_of(s, GROUPS - 1)],
                        i * BANK_TURNS[bank_of(s, GROUPS - 1)] + turns_of_bank(s, GROUPS - 1))

        def copies_of(engine):
            return [(a, b) for a in range(QUADS) if (a >= DVE_QUADS) == engine for b in range(QUADS)]

        DVE_QUADS = 1
        DVE_COPIES, ACT_COPIES = (len(copies_of(k)) for k in range(2))

        @block.sync
        def _(sp):
            def load(i, s):
                at = bass.ds(i * TURN + s * TILE, TILE)
                sp.dma_start(ids_sb[:, s, :], ids[at, :]).then_inc(ids_loaded[s], 16)
                sp.dma_start(rows[:, s, 0, :], dense[at, :]).then_inc(dense_loaded[s], 16)

            def load_wanted(i):
                sp.dma_start(wanted[:, :, :], picked_ids[:, :, bass.ds(i * TURN, TURN)]).then_inc(wanted_loaded, 16)

            load(0, 0)
            load_wanted(0)
            load(0, 1)
            for t in range(PICKS):
                if t >= 2:
                    sp.wait_ge(lo_ready, t - 1)
                table, into = tables[PICKED[t]], raw[:, t % 2, :].rearrange("p (c d) -> p c d", d=DIM)
                sp.dma_start(into[:, 0:WHOLE, :], table[0:P * WHOLE, :].rearrange("(p c) d -> p c d", p=P)
                             ).then_inc(raw_loaded[t % 2], 16)
                sp.wait_ge(raw_cleared, 1)
                sp.dma_start(into[0:REST, WHOLE, :], table[P * WHOLE:SMALL, :]).then_inc(raw_loaded[t % 2], 16)
            with sp.Fori(1, TURNS) as i:
                sp.wait_ge(hot_made, i * PICKS)
                load_wanted(i)
                for s in range(SLOTS):
                    wait_rows_turned(sp, i - 1, s)
                    load(i, s)
            sp.wait_ge(y_kept, TURNS)
            sp.dma_start(out, y[:, :]).then_inc(stored, 16)
            sp.wait_ge(stored, 16)

        @block.gpsimd
        def _(pool):
            pool.memset(ident[:, :], 0.0).then_inc(ident_zeroed, 1)
            pool.wait_ge(ident_zeroed, 1)
            pool.affine_select(out=ident[:, :], in_=ident[:, :], compare_op=ALU.not_equal, fill=1.0,
                               base=0, pattern=[[-1, P]], channel_multiplier=1).then_inc(ident_ready, 1)
            pool.iota(row_int[:, 0:WHOLE], pattern=[[1, WHOLE]], base=0, channel_multiplier=WHOLE).then_inc(rows_numbered, 1)
            pool.iota(row_int[:, WHOLE:PARTS], pattern=[[1, 1]], base=P * WHOLE, channel_multiplier=1
                      ).then_inc(rows_numbered, 1)

            def gather(s):
                for g in range(GROUPS):
                    for n in members(g):
                        if n:
                            pool.indirect_dma_start(
                                out=rows[:, s, n, :], out_offset=None, in_=tables[ORDER[n - 1]],
                                in_offset=bass.IndirectOffsetOnAxis(ap=ids_sb[:, s, n - 1:n], axis=0),
                            ).then_inc(gathered[s][g], 16)

            for s in range(SLOTS):
                pool.wait_ge(ids_loaded[s], 16)
                gather(s)
            with pool.Fori(1, TURNS) as i:
                for s in range(SLOTS):
                    wait_rows_turned(pool, i - 1, s)
                    pool.wait_ge(ids_loaded[s], i * 16 + 16)
                    pool.sem_inc(gathers_begun, 1)
                    gather(s)

        def keep_group(eng, copy, i, s, g):
            k, n = bank_of(s, g), members(g)
            eng.wait_ge(group_turned[k], i * BANK_TURNS[k] + turns_of_bank(s, g))
            copy(cols[:, s, :, n[0]:n[-1] + 1].rearrange("p b n -> p n b"),
                 turned[k][:, 0:len(n), :]).then_inc(group_kept[k], 1)

        def keep_picks(eng, copy, i, g):
            t, k = picks(g), bank_of("pick", g)
            eng.wait_ge(hot_used, i * PICKS + t[-1] + 1)
            n = ROW_FEATURES + t[0]
            copy(cols[:, :, :, n:n + len(t)].rearrange("p s b n -> p n s b"),
                 turned[k][:, :, :].rearrange("p (n s) b -> p n s b", s=SLOTS)[:, 0:len(t)]).then_inc(group_kept[k], 1)

        def keep_z(eng, copy, s, engine, done):
            for a, b in copies_of(engine):
                m = chunks_of_quadrant(b)
                src = gram[s][a * QUAD:a * QUAD + PAIR_ROWS, :, 0:BANK_STEPS * PAIR_COLS]
                src = src.rearrange("p h (t j) -> p h t j", j=PAIR_COLS)[:, :, :, b:b + QUADS * (m - 1) + 1:QUADS]
                at = a * STEPS
                dst = z_raw[b * QUAD:b * QUAD + PAIR_ROWS, 0:m, at:at + STEPS]
                copy(dst.rearrange("p m (h t) -> p h t m", h=2), src).then_inc(done, 1)

        @block.vector
        def _(dve):
            dve.memset(raw[:, :, WHOLE * DIM:PARTS * DIM], 0.0).then_inc(raw_cleared, 1)
            dve.memset(z_raw[:, :, :], 0.0).then_inc(z_zeroed, 1)
            dve.wait_ge(rows_numbered, 2)
            dve.tensor_copy(row_number[:, :], row_int[:, :]).then_inc(numbers_ready, 1)

            def make_hot(i, t):
                if t == 0:
                    dve.wait_ge(wanted_loaded, i * 16 + 16)
                if not isinstance(i, int) or t >= RING:
                    dve.wait_ge(hot_used, i * PICKS + t + 1 - RING)
                for c in range(PARTS):
                    done = dve.tensor_scalar(hot[:, t % RING, c, :], wanted[:, t, :], row_number[:, c:c + 1], None,
                                             ALU.is_equal)
                done.then_inc(hot_made, 1)

            def picked(i, g):
                if bank_of("pick", g) == 0:
                    keep_picks(dve, dve.tensor_copy, i, g)

            def picked_early(i):
                dve.wait_ge(gram_done[SLOTS - 1], i)
                for t in range(RING, PICK_GROUP * EARLY):
                    make_hot(i, t)
                for g in range(EARLY):
                    picked(i, g)

            def picked_late(i):
                for g in range(EARLY, PICK_GROUPS):
                    picked(i, g)

            dve.wait_ge(numbers_ready, 1)
            for t in range(RING):
                make_hot(0, t)
            def split(n):
                whole, hi, lo = of_raw(n)
                if PIECES[n][0] == "dense":
                    dve.wait_ge(raw_loaded[n % 2], loaded(n))
                    dve.tensor_tensor(whole, raw[:, n % 2, 0:HIDDEN1], raw[:, n % 2, HIDDEN1:2 * HIDDEN1],
                                      ALU.add).then_inc(wd_summed, 1)
                dve.wait_ge(hi_ready, n + 1)
                dve.tensor_tensor(lo, whole, hi.bitcast(fp32), ALU.subtract).then_inc(lo_ready, 1)

            for n in range(PICKS):
                split(n)
            dve.wait_ge(z_zeroed, 1)

            def columns(i, s, first=False):
                if not first:
                    dve.wait_ge(gram_done[s], i)
                for g in range(GROUPS):
                    if bank_of(s, g) == 0:
                        keep_group(dve, dve.tensor_copy, i, s, g)

            def interactions(i, s):
                dve.wait_ge(gram_done[s], i + 1)
                if s or not isinstance(i, int):
                    dve.wait_ge(z_lo_kept, i * SLOTS + s)
                keep_z(dve, dve.tensor_copy, s, 0, z_by_dve)
                column = cols[:, s, :, 0]
                dve.tensor_copy(dense_hi[:, s, :], column).then_inc(dense_hi_kept, 1)
                dve.wait_ge(dense_hi_kept, i * SLOTS + s + 1)
                dve.tensor_tensor(dense_lo[:, s, :], column, dense_hi[:, s, :].bitcast(fp32),
                                  ALU.subtract).then_inc(dense_kept, 1)
                dve.wait_ge(z_hi_kept, i * SLOTS + s + 1)
                part = slice(s * TILE, s * TILE + TILE)
                dve.tensor_tensor(z_lo[:, :, part], z_raw[:, :, :], z_hi[:, :, part].bitcast(fp32),
                                  ALU.subtract).then_inc(z_lo_kept, 1)

            for t in range(RING, PICKS):
                make_hot(0, t)
                if t == RING:
                    picked(0, 0)
            for g in range(1, EARLY):
                picked(0, g)
            columns(0, 0, first=True)
            picked_late(0)
            interactions(0, 0)
            for n in range(PICKS, len(PIECES)):
                split(n)
            columns(0, 1, first=True)
            with dve.Fori(1, TURNS) as i:
                for t in range(RING):
                    make_hot(i, t)
                picked_early(i)
                interactions(i - 1, 1)
                columns(i, 0)
                for t in range(PICK_GROUP * EARLY, PICKS):
                    make_hot(i, t)
                picked_late(i)
                columns(i, 1)
                interactions(i, 0)
            interactions(TURNS - 1, 1)

        @block.scalar
        def _(act):
            act.dma_start(b1_sb[:, :], b1).then_inc(loaded_small, 16)
            act.dma_start(b2_sb[:, :], b2).then_inc(loaded_small, 16)
            act.dma_start(w3_sb[:, :], w3).then_inc(loaded_small, 16)
            act.dma_start(w2_sb[:, :, :], w2).then_inc(loaded_w2, 16)
            act.wait_ge(loaded_small, 48)
            act.wait_ge(z_zeroed, 1)

            def copy(dst, src):
                return act.activation(dst, src, ACT.Copy)

            def load_piece(n):
                act.wait_ge(lo_ready, n - 1)
                kind, at = PIECES[n]
                of = w_dense if kind == "dense" else w_pairs[:, at:min(at + 2, ZCHUNKS), :]
                act.dma_start(raw[:, n % 2, 0:of.shape[1] * HIDDEN1].rearrange("p (m n) -> p m n", n=HIDDEN1),
                              of).then_inc(raw_loaded[n % 2], 16)

            def split(n):
                whole, hi, _ = of_raw(n)
                if PIECES[n][0] == "dense":
                    act.wait_ge(wd_summed, 1)
                else:
                    act.wait_ge(raw_loaded[n % 2], loaded(n))
                act.activation(hi, whole, ACT.Copy).then_inc(hi_ready, 1)

            for n in range(PICKS):
                split(n)
            for n in range(PICKS, PICKS + 2):
                load_piece(n)

            def picked(i, groups, first=False):
                if not first:
                    act.wait_ge(gram_done[SLOTS - 1], i)
                    act.wait_ge(dense_kept, i * SLOTS)
                for g in groups:
                    if bank_of("pick", g) == 1:
                        keep_picks(act, copy, i, g)

            def columns(i, s, first=False):
                if not first:
                    act.wait_ge(gram_done[s], i)
                    act.wait_ge(dense_kept, (i - 1) * SLOTS + s + 1)
                for g in range(GROUPS):
                    if bank_of(s, g) == 1:
                        keep_group(act, copy, i, s, g)

            def interactions(i, s):
                act.wait_ge(gram_done[s], i + 1)
                if s or not isinstance(i, int):
                    act.wait_ge(z_lo_kept, i * SLOTS + s)
                keep_z(act, copy, s, 1, z_by_act)
                act.wait_ge(z_by_act, i * (SLOTS * ACT_COPIES) + (s + 1) * ACT_COPIES)
                act.wait_ge(z_by_dve, i * (SLOTS * DVE_COPIES) + (s + 1) * DVE_COPIES)
                act.activation(z_hi[:, :, s * TILE:s * TILE + TILE], z_raw[:, :, :], ACT.Copy).then_inc(z_hi_kept, 1)

            def layer1(i):
                for c in range(K2):
                    act.wait_ge(h1_product, i * K2 + c + 1)
                    act.activation(h1[:, c, :], mlp[c % 2][:, c // 2 * TURN:c // 2 * TURN + TURN],
                                   ACT.Relu, bias=b1_sb[:, c:c + 1]).then_inc(h1_kept, 1)

            def layer2(i):
                for c in range(K3):
                    act.wait_ge(h2_product, i * K3 + c + 1)
                    act.activation(h2[:, c, :], mlp[c][:, 0:TURN], ACT.Relu,
                                   bias=b2_sb[:, c:c + 1]).then_inc(h2_kept, 1)

            def layer3(i):
                act.wait_ge(y_product, i + 1)
                copy(y[0:1, bass.ds(i * TURN, TURN)], mlp[0][0:1, TURN:2 * TURN]).then_inc(y_kept, 1)

            picked(0, range(EARLY), first=True)
            columns(0, 0, first=True)
            picked(0, range(EARLY, PICK_GROUPS), first=True)
            interactions(0, 0)
            for n in range(PICKS, len(PIECES)):
                split(n)
                if n + 2 < len(PIECES):
                    load_piece(n + 2)
            columns(0, 1, first=True)
            with act.Fori(1, TURNS) as i:
                interactions(i - 1, 1)
                picked(i, range(EARLY))
                columns(i, 0)
                layer1(i - 1)
                picked(i, range(EARLY, PICK_GROUPS))
                columns(i, 1)
                interactions(i, 0)
                layer2(i - 1)
                layer3(i - 1)
            interactions(TURNS - 1, 1)
            layer1(TURNS - 1)
            layer2(TURNS - 1)
            layer3(TURNS - 1)

        @block.tensor
        def _(pe):
            pe.wait_ge(ident_ready, 1)

            def pick_columns(i, groups, first):
                for g in groups:
                    k = bank_of("pick", g)
                    if not first or use_of("pick", g):
                        pe.wait_ge(group_kept[k], i * BANK_USES[k] + use_of("pick", g))
                    to = turned[k][:, :, :].rearrange("p (n s) b -> p n (s b)", s=SLOTS)
                    for t in picks(g):
                        if first:
                            pe.wait_ge(lo_ready, t + 1)
                        pe.wait_ge(hot_made, i * PICKS + t + 1)
                        for c in range(PARTS):
                            m = P if c < WHOLE else REST
                            for part in (table_hi, table_lo):
                                done = pe.matmul(to[:, t - picks(g)[0], :], part[0:m, t, c, :], hot[0:m, t % RING, c, :],
                                                 start=(c == 0 and part is table_hi),
                                                 stop=(c == WHOLE and part is table_lo))
                        done.then_inc(hot_used, 1)

            def turn_rows(i, s, first):
                for g in range(GROUPS):
                    k, n = bank_of(s, g), members(g)
                    if g == 0:
                        pe.wait_ge(dense_loaded[s], i * 16 + 16)
                    gathers = sum(f > 0 for f in n)
                    pe.wait_ge(gathered[s][g], i * (16 * gathers) + 16 * gathers)
                    if not first or use_of(s, g):
                        pe.wait_ge(group_kept[k], i * BANK_USES[k] + use_of(s, g))
                    for f in n:
                        done = pe.transpose(turned[k][:, f - n[0], :], rows[:, s, f, :], ident[:, :])
                    done.then_inc(group_turned[k], 1)

            def gram_products(i, s, first):
                for k in range(2):
                    pe.wait_ge(group_kept[k], i * BANK_USES[k] + uses_until(s, k))
                if not first:
                    pe.wait_ge(z_by_dve, (i - 1) * (SLOTS * DVE_COPIES) + (s + 1) * DVE_COPIES)
                    pe.wait_ge(z_by_act, (i - 1) * (SLOTS * ACT_COPIES) + (s + 1) * ACT_COPIES)
                for t in range(STEPS):
                    h, u = divmod(t, BANK_STEPS)
                    for a in range(QUADS):
                        of = cols[:, s, a * STEPS + t, :]
                        done = pe.matmul(gram[s][a * QUAD:a * QUAD + PAIR_ROWS, h, u * PAIR_COLS:(u + 1) * PAIR_COLS],
                                         of[:, 0:PAIR_ROWS], of[:, 1:FEATURES], start=True, stop=True)
                done.then_inc(gram_done[s], 1)

            def layer1(i):
                pe.wait_ge(dense_kept, i * SLOTS + SLOTS)
                pe.wait_ge(z_lo_kept, i * SLOTS + SLOTS)
                for c in range(K2):
                    if c >= 2:
                        pe.wait_ge(h1_kept, i * K2 + c - 1)
                    to = mlp[c % 2][:, c // 2 * TURN:c // 2 * TURN + TURN]
                    n = slice(c * P, c * P + P)
                    sets = [(wd_hi[:, n], wd_lo[:, n], dense_hi[:, :, :].rearrange("p s b -> p (s b)"),
                             dense_lo[:, :, :].rearrange("p s b -> p (s b)"))]
                    for m in range(ZCHUNKS):
                        k = P if m < ZCHUNKS - 1 else LAST_QUADS * QUAD
                        sets.append((wz_hi[0:k, m, n], wz_lo[0:k, m, n], z_hi[0:k, m, :], z_lo[0:k, m, :]))
                    for m, (w_hi, w_lo, x_hi, x_lo) in enumerate(sets):
                        pe.matmul(to, w_hi, x_hi, start=(m == 0), stop=False)
                        pe.matmul(to, w_hi, x_lo, start=False, stop=False)
                        done = pe.matmul(to, w_lo, x_hi, start=False, stop=(m == len(sets) - 1))
                    done.then_inc(h1_product, 1)

            def layer2(i):
                pe.wait_ge(h1_kept, i * K2 + K2)
                for c in range(K3):
                    for m in range(K2):
                        done = pe.matmul(mlp[c][:, 0:TURN], w2_sb[:, m, c * P:c * P + P], h1[:, m, :],
                                         start=(m == 0), stop=(m == K2 - 1))
                    done.then_inc(h2_product, 1)

            def layer3(i):
                pe.wait_ge(h2_kept, i * K3 + K3)
                for m in range(K3):
                    done = pe.matmul(mlp[0][0:1, TURN:2 * TURN], w3_sb[:, m:m + 1], h2[:, m, :],
                                     start=(m == 0), stop=(m == K3 - 1))
                done.then_inc(y_product, 1)

            pick_columns(0, range(EARLY), True)
            turn_rows(0, 0, True)
            pick_columns(0, range(EARLY, PICK_GROUPS), True)
            gram_products(0, 0, True)
            turn_rows(0, 1, True)
            gram_products(0, 1, True)
            pe.wait_ge(lo_ready, len(PIECES))
            pe.wait_ge(loaded_w2, 16)
            pe.wait_ge(loaded_small, 48)
            with pe.Fori(1, TURNS) as i:
                pick_columns(i, range(EARLY), False)
                turn_rows(i, 0, False)
                layer1(i - 1)
                pick_columns(i, range(EARLY, PICK_GROUPS), False)
                turn_rows(i, 1, False)
                gram_products(i, 0, False)
                layer2(i - 1)
                gram_products(i, 1, False)
                layer3(i - 1)
            layer1(TURNS - 1)
            layer2(TURNS - 1)
            layer3(TURNS - 1)


def kernel(**inputs):
    import numpy as np
    import concourse.bacc as bacc
    from concourse.bass_utils import run_bass_kernel_spmd

    w_top1 = np.asarray(inputs["W_top1"])
    w_pairs = np.zeros((P, ZCHUNKS, HIDDEN1), w_top1.dtype)
    place = [0] + [1 + ORDER.index(n) for n in range(TABLES)]
    row = DIM
    for a in range(FEATURES):
        for b in range(a + 1, FEATURES):
            i, j = sorted((place[a], place[b]))
            m, q = divmod(j - 1, QUADS)
            w_pairs[q * QUAD + i, m] = w_top1[row]
            row += 1
    ids = np.asarray(inputs["ids"])
    arrays = {
        "dense": np.ascontiguousarray(inputs["r_dense_features"]),
        "ids": np.ascontiguousarray(ids[:, GATHERED]),
        "picked_ids": np.ascontiguousarray(ids[:, PICKED].T),
        **{f"table{n}": np.ascontiguousarray(inputs[f"tbl_{n}"]) for n in range(TABLES)},
        "w_dense": np.ascontiguousarray(np.stack([w_top1[:DIM], w_top1[row:]], axis=1)),
        "w_pairs": w_pairs,
        "b1": np.ascontiguousarray(np.asarray(inputs["b_top1"]).reshape(-1, P).T),
        "w2": np.ascontiguousarray(np.asarray(inputs["W_top2"]).reshape(-1, P, HIDDEN2).transpose(1, 0, 2)),
        "b2": np.ascontiguousarray(np.asarray(inputs["b_top2"]).reshape(-1, P).T),
        "w3": np.ascontiguousarray(np.asarray(inputs["W_top3"]).reshape(-1, P).T),
    }
    nc = bacc.Bacc("TRN2", target_bir_lowering=False, num_devices=1)
    at = {name: nc.dram_tensor(name, a.shape, mybir.dt.from_np(a.dtype), kind="ExternalInput").ap()
          for name, a in arrays.items()}
    out = nc.dram_tensor("out", (1, BATCH), mybir.dt.float32, kind="ExternalOutput").ap()
    picked_ids = at["picked_ids"].rearrange("(a t) b -> a t b", a=1).to_broadcast([P, PICKS, BATCH])
    dlrm_tower(nc, at["dense"], at["ids"], picked_ids, [at[f"table{n}"] for n in range(TABLES)], at["w_dense"],
               at["w_pairs"], at["b1"], at["w2"], at["b2"], at["w3"], out)
    result = run_bass_kernel_spmd(nc, [arrays], core_ids=[0])
    return result.results[0]["out"].reshape(BATCH, 1)
```

```python
import concourse.bass as bass
from concourse import mybir
from contextlib import ExitStack


BATCH, DIM = 2048, 128
ROWS = [12500, 125000, 12500, 12500, 12500, 1000, 12500, 12500, 1250, 12500, 12500, 1250, 1000,
        1000, 1250, 12500, 1000, 1000, 1000, 1250, 1000, 1000, 1000, 1000, 1000, 1000]
TABLES = len(ROWS)
FEATURES = TABLES + 1
SMALL = 1000
PICKED = [n for n in range(TABLES) if ROWS[n] == SMALL][-9:]
GATHERED = [n for n in range(TABLES) if n not in PICKED]
ORDER = GATHERED + PICKED
HIDDEN1, HIDDEN2 = 512, 256

P = 128
TILE = 128
SLOTS = 2
TURN = SLOTS * TILE
TURNS = BATCH // TURN
BANK = 512
QUAD = 32
QUADS = P // QUAD
GROUP = 4
ROW_FEATURES = 1 + len(GATHERED)
GROUPS = -(-ROW_FEATURES // GROUP)
PICKS = len(PICKED)
PICK_GROUP = 2
PICK_GROUPS = -(-PICKS // PICK_GROUP)
WHOLE = SMALL // P
REST = SMALL - WHOLE * P
PARTS = WHOLE + 1
BANKS = 4
RING = 3
STRIDE = FEATURES + 1
DISTANCES = FEATURES // 2
assert FEATURES == 2 * DISTANCES + 1
STARTS = FEATURES - 1
ZCHUNKS = 3
PER_CHUNK = DISTANCES // ZCHUNKS
WHOLE_PAIRS = PER_CHUNK * STARTS
PAIR_PARTS = WHOLE_PAIRS + DISTANCES
assert DISTANCES == ZCHUNKS * PER_CHUNK + 1 and STARTS == 2 * DISTANCES and PAIR_PARTS <= P
assert ZCHUNKS * PAIR_PARTS == FEATURES * (FEATURES - 1) // 2
PAIR_LOADS = 3
STEPS = TILE // QUADS
BANK_STEPS = STEPS // 2


def pair_number(p, m):
    if p < WHOLE_PAIRS:
        i, d = divmod(p, PER_CHUNK)
        return STRIDE * i + ZCHUNKS * d + m + 1
    i = p - WHOLE_PAIRS
    if m < 2:
        return STRIDE * i + DISTANCES + m
    return STRIDE * (DISTANCES + i) + DISTANCES


def members(g):
    return range(GROUP * g, min(GROUP * (g + 1), ROW_FEATURES))


def picks(g):
    return range(PICK_GROUP * g, min(PICK_GROUP * (g + 1), PICKS))


def dlrm_tower(nc, dense, ids, picked_ids, tables, w_dense, w_pairs, b1, w2, b2, w3, square, out):
    fp32, fp32r, i32 = mybir.dt.float32, mybir.dt.float32r, mybir.dt.int32
    ALU, ACT = mybir.AluOpType, mybir.ActivationFunctionType
    K2, K3 = HIDDEN1 // P, HIDDEN2 // P

    with ExitStack() as ctx:
        def sb(name, shape, dt=fp32):
            return ctx.enter_context(nc.sbuf_tensor(name, shape, dt))

        def pb(name, shape):
            return ctx.enter_context(nc.psum_tensor(name, shape, fp32))

        def sem(name):
            return ctx.enter_context(nc.semaphore(name))

        ids_sb = sb("ids_sb", [P, SLOTS, len(GATHERED)], i32)
        rows = sb("rows", [P, SLOTS, ROW_FEATURES, DIM])
        table_hi = sb("table_hi", [P, PICKS, PARTS, DIM], fp32r)
        table_lo = sb("table_lo", [P, PICKS, PARTS, DIM], fp32r)
        row_int = sb("row_int", [P, PARTS], i32)
        row_number = sb("row_number", [P, PARTS])
        wanted = sb("wanted", [P, PICKS, TURN], i32)
        hot = sb("hot", [P, RING, PARTS, TURN], fp32r)
        cols = sb("cols", [P, SLOTS, TILE, FEATURES])
        dense_hi = sb("dense_hi", [P, SLOTS, TILE], fp32r)
        dense_lo = sb("dense_lo", [P, SLOTS, TILE], fp32r)
        gram_sb = sb("gram_sb", [P, SLOTS, FEATURES, STEPS])
        z_raw = sb("z_raw", [P, SLOTS, ZCHUNKS, TILE])
        z_hi = sb("z_hi", [P, ZCHUNKS, TURN], fp32r)
        z_lo = sb("z_lo", [P, ZCHUNKS, TURN], fp32r)
        h1 = sb("h1", [P, K2, TURN])
        h1_hi = sb("h1_hi", [P, K2, TURN], fp32r)
        h1_lo = sb("h1_lo", [P, K2, TURN], fp32r)
        h2 = sb("h2", [P, K3, TURN])
        y = sb("y", [1, TURN])
        ident = sb("ident", [P, P])
        wd_hi = sb("wd_hi", [P, HIDDEN1], fp32r)
        wd_lo = sb("wd_lo", [P, HIDDEN1], fp32r)
        wz_hi = sb("wz_hi", [P, ZCHUNKS, HIDDEN1], fp32r)
        wz_lo = sb("wz_lo", [P, ZCHUNKS, HIDDEN1], fp32r)
        w2_hi = sb("w2_hi", [P, K2, HIDDEN2], fp32r)
        w2_lo = sb("w2_lo", [P, K2, HIDDEN2], fp32r)
        w3_sb = sb("w3_sb", [P, K3])
        b1_sb = sb("b1_sb", [P, K2])
        b2_sb = sb("b2_sb", [P, K3])

        turned = [pb(f"turned{k}", [P, GROUP, TILE]) for k in range(BANKS)]
        gram = pb("gram", [P, 2, BANK])
        mlp = [pb(f"mlp{k}", [P, BANK]) for k in range(2)]

        ident_zeroed, ident_ready = sem("ident_zeroed"), sem("ident_ready")
        rows_numbered, numbers_ready = sem("rows_numbered"), sem("numbers_ready")
        places_cleared = sem("places_cleared")
        hi_ready, lo_ready = sem("hi_ready"), sem("lo_ready")
        first_wanted_loaded = sem("first_wanted_loaded")
        wanted_loaded, hot_made, hot_used = sem("wanted_loaded"), sem("hot_made"), sem("hot_used")
        gram_cleared = sem("gram_cleared")
        y_free = sem("y_free")
        loaded_small = sem("loaded_small")
        wd_summed = sem("wd_summed")
        ids_loaded = [sem(f"ids_loaded{s}") for s in range(SLOTS)]
        dense_loaded = [sem(f"dense_loaded{s}") for s in range(SLOTS)]
        gathered = [[sem(f"gathered{s}_{g}") for g in range(GROUPS)] for s in range(SLOTS)]
        gathers_begun = sem("gathers_begun")
        group_turned = [sem(f"group_turned{k}") for k in range(BANKS)]
        group_kept = [sem(f"group_kept{k}") for k in range(BANKS)]
        gram_done = [sem(f"gram_done{s}") for s in range(SLOTS)]
        dense_hi_kept, dense_kept = sem("dense_hi_kept"), sem("dense_kept")
        z_hi_kept, z_lo_kept = sem("z_hi_kept"), sem("z_lo_kept")
        gram_kept = [sem(f"gram_kept{h}") for h in range(2)]
        square_written = sem("square_written")
        z_loaded = [sem(f"z_loaded{s}") for s in range(SLOTS)]
        h1_product, h2_product, y_product = sem("h1_product"), sem("h2_product"), sem("y_product")
        h1_kept, h2_kept = sem("h1_kept"), sem("h2_kept")
        h1_lo_kept = sem("h1_lo_kept")
        y_kept = sem("y_kept")

        block = ctx.enter_context(nc.Block())

        def half_bank(c):
            return slice(c // 2 * TURN, c // 2 * TURN + TURN)

        def is_first(i):
            return isinstance(i, int) and i == 0

        EARLY = 3
        EARLY_PICKS = PICK_GROUP * EARLY
        assert PICK_GROUPS - EARLY <= BANKS and RING <= EARLY_PICKS < PICKS

        USES = [("pick", g) for g in range(EARLY)] + [(0, g) for g in range(GROUPS)]
        USES += [("pick", g) for g in range(EARLY, PICK_GROUPS)] + [(1, g) for g in range(GROUPS)]
        BANK_USES = [len(USES[k::BANKS]) for k in range(BANKS)]

        def bank_of(s, g):
            return USES.index((s, g)) % BANKS

        GROUPS_OF_DVE, GROUPS_OF_ACT = range(1, GROUPS, 2), range(0, GROUPS, 2)

        def use_of(s, g):
            return USES.index((s, g)) // BANKS

        def uses_until(s, k):
            last = ("pick", PICK_GROUPS - 1) if s == 0 else (s, GROUPS - 1)
            return len(USES[k:USES.index(last) + 1:BANKS])

        def turns_of_bank(s, g):
            k = bank_of(s, g)
            return sum(u[0] != "pick" for u in USES[k:USES.index((s, g)) + 1:BANKS])

        BANK_TURNS = [sum(u[0] != "pick" for u in USES[k::BANKS]) for k in range(BANKS)]

        def piece(kind, place, hi, lo):
            return {"kind": kind, "place": place, "hi": hi, "lo": lo}

        COLS_TABLES = SLOTS * TILE * FEATURES // (PARTS * DIM)
        ROWS_TABLES = ROW_FEATURES // PARTS
        cols_flat = cols[:, :, :, :].rearrange("p s b n -> p (s b n)")[:, 0:COLS_TABLES * PARTS * DIM]
        cols_tables = cols_flat.rearrange("p (t c d) -> p t c d", t=COLS_TABLES, d=DIM)
        rows_tables = rows[:, SLOTS - 1, 0:ROWS_TABLES * PARTS, :].rearrange("p (t c) d -> p t c d", t=ROWS_TABLES)
        h1_table = h1[:, :, :].rearrange("p k b -> p (k b)").rearrange("p (c d) -> p c d", d=DIM)
        assert PICKS <= ROWS_TABLES + COLS_TABLES + 1 and K2 * TURN == PARTS * DIM
        table_at = [rows_tables[:, t] for t in range(ROWS_TABLES)]
        table_at += [cols_tables[:, t] for t in range(COLS_TABLES)] + [h1_table]
        squares_flat = gram_sb[:, :, :, :].rearrange("p s j t -> p (s j t)")
        pairs_at = squares_flat[0:PAIR_PARTS, 0:ZCHUNKS * HIDDEN1].rearrange("p (m n) -> p m n", n=HIDDEN1)
        wd_at = [h2[:, :, :].rearrange("p k b -> p (k b)"),
                 z_raw[:, :, :, :].rearrange("p s m b -> p (s m b)")[:, 0:HIDDEN1]]
        wd_raw = wd_at[0]
        PIECES = [piece("table", table_at[t], table_hi[:, t], table_lo[:, t]) for t in range(PICKS)]
        PIECES.append(piece("pairs", pairs_at, wz_hi[0:PAIR_PARTS], wz_lo[0:PAIR_PARTS]))
        PIECES.append(piece("dense", wd_raw, wd_hi[:, :], wd_lo[:, :]))
        PIECES.append(piece("w2", h1[:, :, :], w2_hi[:, :, :], w2_lo[:, :, :]))
        PAIRS_PIECE, DENSE_PIECE, W2_PIECE = range(PICKS, len(PIECES))
        piece_loaded = [sem(f"piece_loaded{n}") for n in range(len(PIECES))]

        def wait_rows_turned(eng, i, s):
            eng.wait_ge(group_turned[bank_of(s, GROUPS - 1)],
                        i * BANK_TURNS[bank_of(s, GROUPS - 1)] + turns_of_bank(s, GROUPS - 1))

        @block.sync
        def _(sp):
            def load(i, s, ahead=0):
                at = bass.ds(i * TURN + (ahead * TURN + s * TILE), TILE)
                sp.dma_start(ids_sb[:, s, :], ids[at, :]).then_inc(ids_loaded[s], 16)
                sp.dma_start(rows[:, s, 0, :], dense[at, :]).then_inc(dense_loaded[s], 16)

            def load_wanted(i, ahead=0):
                at = bass.ds((i + ahead) * TURN, TURN)
                sp.dma_start(wanted[:, :, :], picked_ids[:, :, at]).then_inc(wanted_loaded, 16)

            def pairs_of_square(i, s):
                n = i * SLOTS + s
                sp.wait_ge(gram_kept[1], n + 1)
                for a in range(QUADS):
                    of = square[s, 0:FEATURES * FEATURES, a * STEPS:a * STEPS + STEPS]
                    sp.dma_start(of.rearrange("(i j) t -> i j t", j=FEATURES),
                                 gram_sb[a * QUAD:a * QUAD + FEATURES, s]).then_inc(square_written, 16)
                sp.wait_ge(square_written, n * (16 * QUADS) + 16 * QUADS)
                number = square[s, 0:STARTS * STRIDE, :].rearrange("(i d) b -> i d b", d=STRIDE)
                sp.dma_start(z_raw[0:WHOLE_PAIRS, s, :, :], number[:, 1:DISTANCES, :]).then_inc(z_loaded[s], 16)
                sp.dma_start(z_raw[WHOLE_PAIRS:PAIR_PARTS, s, 0:2, :], number[0:DISTANCES, DISTANCES:DISTANCES + 2, :]
                             ).then_inc(z_loaded[s], 16)
                sp.dma_start(z_raw[WHOLE_PAIRS:PAIR_PARTS, s, 2, :], number[DISTANCES:STARTS, DISTANCES, :]
                             ).then_inc(z_loaded[s], 16)

            load(0, 0)
            sp.dma_start(wanted[:, 0:RING, :], picked_ids[:, 0:RING, 0:TURN]).then_inc(first_wanted_loaded, 16)
            sp.wait_ge(places_cleared, 3)
            for t in range(PICKS):
                table, into = tables[PICKED[t]], PIECES[t]["place"]
                sp.dma_start(into[:, 0:WHOLE, :], table[0:P * WHOLE, :].rearrange("(p c) d -> p c d", p=P)
                             ).then_inc(piece_loaded[t], 16)
                sp.dma_start(into[0:REST, WHOLE, :], table[P * WHOLE:SMALL, :]).then_inc(piece_loaded[t], 16)
                if t == 0:
                    sp.dma_start(wanted[:, RING:PICKS, :], picked_ids[:, RING:PICKS, 0:TURN]
                                 ).then_inc(wanted_loaded, 16)
            sp.wait_ge(lo_ready, ROWS_TABLES)
            load(0, 1)

            def next_loads(i):
                wait_rows_turned(sp, i, 0)
                load(i, 0, ahead=1)
                sp.wait_ge(hot_made, i * PICKS + PICKS)
                load_wanted(i, ahead=1)
                wait_rows_turned(sp, i, 1)
                load(i, 1, ahead=1)

            def squares(i):
                for s in range(SLOTS):
                    pairs_of_square(i, s)

            def store_before(i):
                sp.wait_ge(y_kept, i)
                sp.dma_start(out[:, bass.ds(i * TURN - TURN, TURN)], y[:, :]).then_inc(y_free, 16)

            next_loads(0)
            squares(0)
            with sp.Fori(1, TURNS - 1) as i:
                next_loads(i)
                squares(i)
                store_before(i)
            squares(TURNS - 1)
            store_before(TURNS - 1)
            store_before(TURNS)
            sp.wait_ge(y_free, TURNS * 16 + 16)

        @block.gpsimd
        def _(pool):
            pool.memset(ident[:, :], 0.0).then_inc(ident_zeroed, 1)
            pool.wait_ge(ident_zeroed, 1)
            pool.affine_select(out=ident[:, :], in_=ident[:, :], compare_op=ALU.not_equal, fill=1.0,
                               base=0, pattern=[[-1, P]], channel_multiplier=1).then_inc(ident_ready, 1)
            pool.iota(row_int[:, 0:WHOLE], pattern=[[1, WHOLE]], base=0, channel_multiplier=WHOLE
                      ).then_inc(rows_numbered, 1)
            pool.iota(row_int[:, WHOLE:PARTS], pattern=[[1, 1]], base=P * WHOLE, channel_multiplier=1
                      ).then_inc(rows_numbered, 1)

            def gather(s):
                for g in range(GROUPS):
                    for n in members(g):
                        if n:
                            pool.indirect_dma_start(
                                out=rows[:, s, n, :], out_offset=None, in_=tables[ORDER[n - 1]],
                                in_offset=bass.IndirectOffsetOnAxis(ap=ids_sb[:, s, n - 1:n], axis=0),
                            ).then_inc(gathered[s][g], 16)

            for s in range(SLOTS):
                pool.wait_ge(ids_loaded[s], 16)
                if s == SLOTS - 1:
                    pool.wait_ge(lo_ready, ROWS_TABLES)
                gather(s)
            with pool.Fori(1, TURNS) as i:
                for s in range(SLOTS):
                    wait_rows_turned(pool, i - 1, s)
                    pool.wait_ge(ids_loaded[s], i * 16 + 16)
                    pool.sem_inc(gathers_begun, 1)
                    gather(s)

        def keep_group(eng, copy, i, s, g):
            k, n = bank_of(s, g), members(g)
            eng.wait_ge(group_turned[k], i * BANK_TURNS[k] + turns_of_bank(s, g))
            copy(cols[:, s, :, n[0]:n[-1] + 1].rearrange("p b n -> p n b"),
                 turned[k][:, 0:len(n), :]).then_inc(group_kept[k], 1)

        def keep_picks(eng, copy, i, g):
            t, k = picks(g), bank_of("pick", g)
            eng.wait_ge(hot_used, i * PICKS + t[-1] + 1)
            n = ROW_FEATURES + t[0]
            copy(cols[:, :, :, n:n + len(t)].rearrange("p s b n -> p n s b"),
                 turned[k][:, :, :].rearrange("p (n s) b -> p n s b", s=SLOTS)[:, 0:len(t)]).then_inc(group_kept[k], 1)

        def keep_gram(eng, copy, i, s, h):
            eng.wait_ge(gram_done[s], i * 2 + (h + 1))
            if h == 1:
                eng.wait_ge(gram_kept[0], i * SLOTS + (s + 1))
            copy(gram_sb[:, s, :, h * BANK_STEPS:(h + 1) * BANK_STEPS].rearrange("p j t -> p t j"),
                 gram[:, h, 0:BANK_STEPS * FEATURES].rearrange("p (t j) -> p t j", j=FEATURES)
                 ).then_inc(gram_kept[h], 1)

        @block.vector
        def _(dve):
            dve.memset(cols_tables[:, :, WHOLE, :], 0.0).then_inc(places_cleared, 1)
            dve.memset(h1_table[:, WHOLE, :], 0.0).then_inc(places_cleared, 1)
            dve.memset(rows_tables[:, :, WHOLE, :], 0.0).then_inc(places_cleared, 1)
            dve.memset(gram[:, :, :], 0.0).then_inc(gram_cleared, 1)
            dve.memset(y[:, :], 0.0).then_inc(y_free, 16)
            dve.wait_ge(rows_numbered, 2)
            dve.tensor_copy(row_number[:, :], row_int[:, :]).then_inc(numbers_ready, 1)

            def make_hot(i, t):
                if t == 0 and is_first(i):
                    dve.wait_ge(first_wanted_loaded, 16)
                if t == (RING if is_first(i) else 0):
                    dve.wait_ge(wanted_loaded, i * 16 + 16)
                if not is_first(i) or t >= RING:
                    dve.wait_ge(hot_used, i * PICKS + t + 1 - RING)
                for c in range(PARTS):
                    done = dve.tensor_scalar(hot[:, t % RING, c, :], wanted[:, t, :], row_number[:, c:c + 1], None,
                                             ALU.is_equal)
                done.then_inc(hot_made, 1)

            def split(n):
                piece = PIECES[n]
                whole = piece["place"]
                if piece["kind"] == "dense":
                    dve.wait_ge(piece_loaded[n], 32)
                    dve.tensor_tensor(wd_raw, wd_at[0], wd_at[1], ALU.add).then_inc(wd_summed, 1)
                dve.wait_ge(hi_ready, n + 1)
                dve.tensor_tensor(piece["lo"], whole, piece["hi"].bitcast(fp32), ALU.subtract).then_inc(lo_ready, 1)

            dve.wait_ge(numbers_ready, 1)
            for t in range(PICKS):
                if t < EARLY_PICKS:
                    make_hot(0, t)
                split(t)

            def columns(i, s, first=False):
                if not first:
                    dve.wait_ge(gram_done[s], i * 2)
                for g in GROUPS_OF_DVE:
                    keep_group(dve, dve.tensor_copy, i, s, g)

            def dense_parts(i, s):
                column = cols[:, s, :, 0]
                dve.tensor_copy(dense_hi[:, s, :], column).then_inc(dense_hi_kept, 1)
                dve.wait_ge(dense_hi_kept, i * SLOTS + s + 1)
                dve.tensor_tensor(dense_lo[:, s, :], column, dense_hi[:, s, :].bitcast(fp32),
                                  ALU.subtract).then_inc(dense_kept, 1)

            def low_parts(i, s):
                part = slice(s * TILE, s * TILE + TILE)
                dve.wait_ge(z_hi_kept, i * SLOTS + s + 1)
                dve.tensor_tensor(z_lo[0:PAIR_PARTS, :, part], z_raw[0:PAIR_PARTS, s, :, :],
                                  z_hi[0:PAIR_PARTS, :, part].bitcast(fp32), ALU.subtract).then_inc(z_lo_kept, 1)

            def square_kept(i, s):
                keep_gram(dve, dve.tensor_copy, i, s, 1)

            def h1_low_parts(n):
                for c in range(K2):
                    dve.wait_ge(h1_kept, n * K2 + c + 1)
                    dve.tensor_tensor(h1_lo[:, c, :], h1[:, c, :], h1_hi[:, c, :].bitcast(fp32),
                                      ALU.subtract).then_inc(h1_lo_kept, 1)

            dve.wait_ge(lo_ready, PICKS)
            make_hot(0, EARLY_PICKS)
            columns(0, 0, first=True)
            for t in range(EARLY_PICKS + 1, PICKS):
                make_hot(0, t)
            for n in (PAIRS_PIECE, DENSE_PIECE, W2_PIECE):
                split(n)
            columns(0, 1, first=True)

            def turn(i, last=False):
                make_hot(i, 0)
                square_kept(i - 1, 0)
                for t in range(1, RING):
                    make_hot(i, t)
                square_kept(i - 1, 1)
                for s in range(SLOTS):
                    dense_parts(i - 1, s)
                for t in range(RING, EARLY_PICKS):
                    make_hot(i, t)
                low_parts(i - 1, 0)
                make_hot(i, EARLY_PICKS)
                low_parts(i - 1, 1)
                columns(i, 0)
                for t in range(EARLY_PICKS + 1, PICKS):
                    make_hot(i, t)
                if last:
                    square_kept(i, 0)
                else:
                    h1_low_parts(i - 1)
                columns(i, 1)

            with dve.Fori(1, TURNS - 1) as i:
                turn(i)
            turn(TURNS - 1, last=True)
            square_kept(TURNS - 1, 1)
            dve.wait_ge(h1_product, (TURNS - 1) * K2)
            for s in range(SLOTS):
                dense_parts(TURNS - 1, s)
            h1_low_parts(TURNS - 2)
            for s in range(SLOTS):
                low_parts(TURNS - 1, s)
            h1_low_parts(TURNS - 1)

        @block.scalar
        def _(act):
            def copy(dst, src):
                return act.activation(dst, src, ACT.Copy)

            def load_weights(n):
                piece = PIECES[n]
                if piece["kind"] == "dense":
                    for k in range(2):
                        act.dma_start(wd_at[k], w_dense[:, k, :]).then_inc(piece_loaded[n], 16)
                else:
                    of = w2 if piece["kind"] == "w2" else w_pairs
                    act.dma_start(piece["place"], of).then_inc(piece_loaded[n], 16)

            def split(n):
                piece = PIECES[n]
                whole = piece["place"]
                if piece["kind"] == "dense":
                    act.wait_ge(wd_summed, 1)
                else:
                    act.wait_ge(piece_loaded[n], 32 if piece["kind"] == "table" else 16)
                act.activation(piece["hi"], whole, ACT.Copy).then_inc(hi_ready, 1)

            for n in range(PICKS):
                split(n)
            for n in (PAIRS_PIECE, DENSE_PIECE):
                load_weights(n)
            act.dma_start(b1_sb[:, :], b1).then_inc(loaded_small, 16)
            act.dma_start(b2_sb[:, :], b2).then_inc(loaded_small, 16)
            act.dma_start(w3_sb[:, :], w3).then_inc(loaded_small, 16)

            def picked(i, groups, first=False):
                if not first:
                    act.wait_ge(gram_done[SLOTS - 1], i * 2)
                for g in groups:
                    keep_picks(act, copy, i, g)

            def columns(i, s, first=False):
                if not first:
                    act.wait_ge(gram_done[s], i * 2)
                    act.wait_ge(dense_kept, (i - 1) * SLOTS + s + 1)
                for g in GROUPS_OF_ACT:
                    keep_group(act, copy, i, s, g)

            def square_kept(i, s):
                keep_gram(act, copy, i, s, 0)

            def high_parts(i, s):
                act.wait_ge(z_loaded[s], i * (16 * PAIR_LOADS) + 16 * PAIR_LOADS)
                act.activation(z_hi[0:PAIR_PARTS, :, s * TILE:s * TILE + TILE], z_raw[0:PAIR_PARTS, s, :, :],
                               ACT.Copy).then_inc(z_hi_kept, 1)

            def layer1(n):
                for c in range(K2):
                    act.wait_ge(h1_product, n * K2 + c + 1)
                    act.activation(h1_hi[:, c, :], mlp[c % 2][:, half_bank(c)], ACT.Relu, bias=b1_sb[:, c:c + 1])
                    act.activation(h1[:, c, :], mlp[c % 2][:, half_bank(c)],
                                   ACT.Relu, bias=b1_sb[:, c:c + 1]).then_inc(h1_kept, 1)

            def layer2(n):
                for c in range(K3):
                    act.wait_ge(h2_product, n * K3 + c + 1)
                    act.activation(h2[:, c, :], mlp[c][:, 0:TURN], ACT.Relu,
                                   bias=b2_sb[:, c:c + 1]).then_inc(h2_kept, 1)

            def layer3(n):
                act.wait_ge(y_product, n + 1)
                act.wait_ge(y_free, n * 16 + 16)
                copy(y[:, :], mlp[0][0:1, half_bank(2)]).then_inc(y_kept, 1)

            act.wait_ge(lo_ready, PICKS)
            load_weights(W2_PIECE)
            picked(0, range(EARLY), first=True)
            columns(0, 0, first=True)
            split(PAIRS_PIECE)
            picked(0, range(EARLY, PICK_GROUPS), first=True)
            for n in (DENSE_PIECE, W2_PIECE):
                split(n)
            act.wait_ge(lo_ready, W2_PIECE)
            square_kept(0, 0)
            columns(0, 1, first=True)
            act.wait_ge(loaded_small, 48)

            def turn(i, last=False):
                square_kept(i - 1, 1)
                high_parts(i - 1, 0)
                picked(i, range(EARLY))
                high_parts(i - 1, 1)
                columns(i, 0)
                if not last:
                    layer1(i - 1)
                picked(i, range(EARLY, PICK_GROUPS))
                if last:
                    square_kept(i, 0)
                columns(i, 1)
                if last:
                    square_kept(i, 1)
                    layer1(i - 1)
                else:
                    square_kept(i, 0)
                layer2(i - 1)
                layer3(i - 1)

            with act.Fori(1, TURNS - 1) as i:
                turn(i)
            turn(TURNS - 1, last=True)
            for s in range(SLOTS):
                high_parts(TURNS - 1, s)
            layer1(TURNS - 1)
            layer2(TURNS - 1)
            layer3(TURNS - 1)

        @block.tensor
        def _(pe):
            pe.wait_ge(ident_ready, 1)
            pe.wait_ge(gram_cleared, 1)

            def pick_columns(i, groups, first):
                for g in groups:
                    k = bank_of("pick", g)
                    if not first or use_of("pick", g):
                        pe.wait_ge(group_kept[k], i * BANK_USES[k] + use_of("pick", g))
                    to = turned[k][:, :, :].rearrange("p (n s) b -> p n (s b)", s=SLOTS)
                    for t in picks(g):
                        if first:
                            pe.wait_ge(lo_ready, t + 1)
                        pe.wait_ge(hot_made, i * PICKS + t + 1)
                        for c in range(PARTS):
                            m = P if c < WHOLE else REST
                            for part in (table_hi, table_lo):
                                done = pe.matmul(to[:, t - picks(g)[0], :], part[0:m, t, c, :],
                                                 hot[0:m, t % RING, c, :],
                                                 start=(c == 0 and part is table_hi),
                                                 stop=(c == WHOLE and part is table_lo))
                        done.then_inc(hot_used, 1)

            def turn_rows(i, s, first):
                for g in range(GROUPS):
                    k, n = bank_of(s, g), members(g)
                    if g == 0:
                        pe.wait_ge(dense_loaded[s], i * 16 + 16)
                    gathers = sum(f > 0 for f in n)
                    pe.wait_ge(gathered[s][g], i * (16 * gathers) + 16 * gathers)
                    if not first or use_of(s, g):
                        pe.wait_ge(group_kept[k], i * BANK_USES[k] + use_of(s, g))
                    for f in n:
                        done = pe.transpose(turned[k][:, f - n[0], :], rows[:, s, f, :], ident[:, :])
                    done.then_inc(group_turned[k], 1)

            def gram_products(i, s, first):
                for k in range(BANKS):
                    pe.wait_ge(group_kept[k], i * BANK_USES[k] + uses_until(s, k))
                for h in range(2):
                    if s or not first:
                        pe.wait_ge(gram_kept[h], i * SLOTS + s)
                    for u in range(BANK_STEPS):
                        for a in range(QUADS):
                            of = cols[:, s, a * STEPS + h * BANK_STEPS + u, :]
                            done = pe.matmul(gram[a * QUAD:a * QUAD + FEATURES, h, u * FEATURES:(u + 1) * FEATURES],
                                             of, of, start=True, stop=True)
                    done.then_inc(gram_done[s], 1)

            def layer1(n):
                pe.wait_ge(z_hi_kept, n * SLOTS + SLOTS)
                pe.wait_ge(dense_kept, n * SLOTS + SLOTS)
                for c in range(K2):
                    if c >= 2:
                        pe.wait_ge(h1_kept, n * K2 + c - 1)
                    to = mlp[c % 2][:, half_bank(c)]
                    of = slice(c * P, c * P + P)
                    sets = [(wd_hi[:, of], wd_lo[:, of], dense_hi[:, :, :].rearrange("p s b -> p (s b)"),
                             dense_lo[:, :, :].rearrange("p s b -> p (s b)"))]
                    k = slice(0, PAIR_PARTS)
                    sets += [(wz_hi[k, m, of], wz_lo[k, m, of], z_hi[k, m, :], z_lo[k, m, :]) for m in range(ZCHUNKS)]
                    for m, (w_hi, w_lo, x_hi, x_lo) in enumerate(sets):
                        pe.matmul(to, w_hi, x_hi, start=(m == 0), stop=False)
                        pe.matmul(to, w_lo, x_hi, start=False, stop=False)
                    if c == 0:
                        pe.wait_ge(z_lo_kept, n * SLOTS + SLOTS)
                    for m, (w_hi, w_lo, x_hi, x_lo) in enumerate(sets):
                        done = pe.matmul(to, w_hi, x_lo, start=False, stop=(m == len(sets) - 1))
                    done.then_inc(h1_product, 1)

            def layer2(n):
                pe.wait_ge(h1_kept, n * K2 + K2 - 1)
                for c in range(K3):
                    of = slice(c * P, c * P + P)
                    for m in range(K2):
                        if c == 0 and m == K2 - 1:
                            pe.wait_ge(h1_kept, n * K2 + K2)
                        pe.matmul(mlp[c][:, 0:TURN], w2_hi[:, m, of], h1_hi[:, m, :], start=(m == 0), stop=False)
                        pe.matmul(mlp[c][:, 0:TURN], w2_lo[:, m, of], h1_hi[:, m, :], start=False, stop=False)
                    for m in range(K2):
                        if c == 0:
                            pe.wait_ge(h1_lo_kept, n * K2 + m + 1)
                        done = pe.matmul(mlp[c][:, 0:TURN], w2_hi[:, m, of], h1_lo[:, m, :],
                                         start=False, stop=(m == K2 - 1))
                    done.then_inc(h2_product, 1)

            def layer3(n):
                for m in range(K3):
                    pe.wait_ge(h2_kept, n * K3 + m + 1)
                    done = pe.matmul(mlp[0][0:1, half_bank(2)], w3_sb[:, m:m + 1], h2[:, m, :],
                                     start=(m == 0), stop=(m == K3 - 1))
                done.then_inc(y_product, 1)

            pick_columns(0, range(EARLY), True)
            turn_rows(0, 0, True)
            pick_columns(0, range(EARLY, PICK_GROUPS), True)
            gram_products(0, 0, True)
            turn_rows(0, 1, True)
            gram_products(0, 1, True)
            pe.wait_ge(lo_ready, len(PIECES))
            pe.wait_ge(loaded_small, 48)
            with pe.Fori(1, TURNS - 1) as i:
                pick_columns(i, range(EARLY), False)
                turn_rows(i, 0, False)
                layer1(i - 1)
                pick_columns(i, range(EARLY, PICK_GROUPS), False)
                turn_rows(i, 1, False)
                gram_products(i, 0, False)
                layer2(i - 1)
                gram_products(i, 1, False)
                layer3(i - 1)
            pick_columns(TURNS - 1, range(EARLY), False)
            turn_rows(TURNS - 1, 0, False)
            pick_columns(TURNS - 1, range(EARLY, PICK_GROUPS), False)
            gram_products(TURNS - 1, 0, False)
            turn_rows(TURNS - 1, 1, False)
            gram_products(TURNS - 1, 1, False)
            layer1(TURNS - 2)
            layer2(TURNS - 2)
            layer3(TURNS - 2)
            layer1(TURNS - 1)
            layer2(TURNS - 1)
            layer3(TURNS - 1)


def kernel(**inputs):
    import numpy as np
    import concourse.bacc as bacc
    from concourse.bass_utils import run_bass_kernel_spmd

    w_top1 = np.asarray(inputs["W_top1"])
    place = [0] + [1 + ORDER.index(n) for n in range(TABLES)]
    row_of = {}
    for a in range(FEATURES):
        for b in range(a + 1, FEATURES):
            row_of[frozenset((place[a], place[b]))] = DIM + len(row_of)
    pairs = [[row_of[frozenset(divmod(pair_number(p, m), FEATURES))] for m in range(ZCHUNKS)]
             for p in range(PAIR_PARTS)]
    assert sorted(sum(pairs, [])) == sorted(row_of.values())
    w_pairs = np.ascontiguousarray(w_top1[np.asarray(pairs)])
    dense_again = DIM + len(row_of)
    ids = np.asarray(inputs["ids"])
    arrays = {
        "dense": np.ascontiguousarray(inputs["r_dense_features"]),
        "ids": np.ascontiguousarray(ids[:, GATHERED]),
        "picked_ids": np.ascontiguousarray(ids[:, PICKED].T),
        **{f"table{n}": np.ascontiguousarray(inputs[f"tbl_{n}"]) for n in range(TABLES)},
        "w_dense": np.ascontiguousarray(np.stack([w_top1[:DIM], w_top1[dense_again:]], axis=1)),
        "w_pairs": w_pairs,
        "b1": np.ascontiguousarray(np.asarray(inputs["b_top1"]).reshape(-1, P).T),
        "w2": np.ascontiguousarray(np.asarray(inputs["W_top2"]).reshape(-1, P, HIDDEN2).transpose(1, 0, 2)),
        "b2": np.ascontiguousarray(np.asarray(inputs["b_top2"]).reshape(-1, P).T),
        "w3": np.ascontiguousarray(np.asarray(inputs["W_top3"]).reshape(-1, P).T),
    }
    nc = bacc.Bacc("TRN2", target_bir_lowering=False, num_devices=1)
    at = {name: nc.dram_tensor(name, a.shape, mybir.dt.from_np(a.dtype), kind="ExternalInput").ap()
          for name, a in arrays.items()}
    out = nc.dram_tensor("out", (1, BATCH), mybir.dt.float32, kind="ExternalOutput").ap()
    picked_ids = at["picked_ids"].rearrange("(a t) b -> a t b", a=1).to_broadcast([P, PICKS, BATCH])
    square = nc.dram_tensor("square", (SLOTS, STARTS * STRIDE + STRIDE, TILE), mybir.dt.float32).ap()
    dlrm_tower(nc, at["dense"], at["ids"], picked_ids, [at[f"table{n}"] for n in range(TABLES)], at["w_dense"],
               at["w_pairs"], at["b1"], at["w2"], at["b2"], at["w3"], square, out)
    result = run_bass_kernel_spmd(nc, [arrays], core_ids=[0])
    return result.results[0]["out"].reshape(BATCH, 1)
```
